# Optimizing a Trainium2 kernel written in Bass

```python
import numpy as np
import jax
import jax.numpy as jnp

def _softmax(x, axis=-1):
    return jax.nn.softmax(x, axis=axis)

def _gelu(x):
    return jax.nn.gelu(x, approximate=True)

def _silu(x):
    return jax.nn.silu(x)

def _sigmoid(x):
    return jax.nn.sigmoid(x)

def _layernorm(x, axis=-1, eps=1e-05):
    m = jnp.mean(x, axis=axis, keepdims=True)
    v = jnp.var(x, axis=axis, keepdims=True)
    return (x - m) / jnp.sqrt(v + eps)

def _scatter_add(tgt, idx, src, axis=0):
    return tgt.at[idx].add(src)

def _segment_sum(src, seg, n):
    return jax.ops.segment_sum(src, seg, n)
kernel_name = 'mk_gnn_preln_d2_gnn_r8_378f46'

def setup_inputs(seed: int=0):
    np.random.seed(seed)
    _w = jnp.asarray

    def _rec_inputs():
        import jax
        import jax.numpy as jnp
        _gk = jax.random.key(seed)
        x = -0.000202 + 1 * jax.random.normal(jax.random.fold_in(_gk, 1), (6250, 128), jnp.float32)
        src = jax.random.randint(jax.random.fold_in(_gk, 2), (200000,), 0, 6250, jnp.int32)
        dst = jax.random.randint(jax.random.fold_in(_gk, 3), (200000,), 0, 6250, jnp.int32)
        _o = jnp.argsort(dst, stable=True)
        src = src[_o]
        dst = dst[_o]
        edge_attr_128 = 2.93046e-05 + 1.00006 * jax.random.normal(jax.random.fold_in(_gk, 11), (200000, 128), jnp.float32)
        return (x, src, dst, edge_attr_128)
    x, src, dst, edge_attr_128 = _rec_inputs()

    def _L0_gnn_setup():
        import jax, jax.numpy as jnp
        import numpy as np
        N_NODES = 6250
        N_EDGES = 80000
        HID = 128
        LN_EPS = 1e-05

        def _layer_norm(h, gamma, beta):
            mu = jnp.mean(h, axis=-1, keepdims=True)
            var = jnp.mean(jnp.square(h - mu), axis=-1, keepdims=True)
            return (h - mu) * jax.lax.rsqrt(var + LN_EPS) * gamma + beta
        key = jax.random.key(seed)
        ks = jax.random.split(key, 8)
        x = jax.random.normal(ks[0], (N_NODES, HID), dtype=jnp.float32)
        edge_index = jax.random.randint(ks[1], (2, N_EDGES), 0, N_NODES, dtype=jnp.int64)
        edge_attr = jax.random.normal(ks[2], (N_EDGES, HID), dtype=jnp.float32)
        msg_W1 = jax.random.normal(ks[3], (3 * HID, HID), dtype=jnp.float32) / np.sqrt(3 * HID)
        msg_b1 = jnp.zeros((HID,), dtype=jnp.float32)
        msg_W2 = jax.random.normal(ks[4], (HID, HID), dtype=jnp.float32) / np.sqrt(HID)
        msg_b2 = jnp.zeros((HID,), dtype=jnp.float32)
        upd_W1 = jax.random.normal(ks[5], (2 * HID, HID), dtype=jnp.float32) / np.sqrt(2 * HID)
        upd_b1 = jnp.zeros((HID,), dtype=jnp.float32)
        upd_W2 = jax.random.normal(ks[6], (HID, HID), dtype=jnp.float32) / np.sqrt(HID)
        upd_b2 = jnp.zeros((HID,), dtype=jnp.float32)
        ln_gamma = jnp.ones((HID,), dtype=jnp.float32)
        ln_beta = jnp.zeros((HID,), dtype=jnp.float32)
        return {'x': x, 'edge_index': edge_index, 'edge_attr': edge_attr, 'msg_W1': msg_W1, 'msg_b1': msg_b1, 'msg_W2': msg_W2, 'msg_b2': msg_b2, 'upd_W1': upd_W1, 'upd_b1': upd_b1, 'upd_W2': upd_W2, 'upd_b2': upd_b2, 'ln_gamma': ln_gamma, 'ln_beta': ln_beta}
    _L0_gnn_all = _L0_gnn_setup()
    _L0_gnn_in = {k: v for k, v in _L0_gnn_all.items() if k in ('msg_W1', 'msg_b1', 'msg_W2', 'msg_b2', 'upd_W1', 'upd_b1', 'upd_W2', 'upd_b2', 'ln_gamma', 'ln_beta')}
    del _L0_gnn_all

    def _L1_gnn_setup():
        import jax, jax.numpy as jnp
        import numpy as np
        N = 6250
        E = 75000
        H = 4
        C = 32
        IN = 128
        NEG_SLOPE = 0.2
        key = jax.random.key(seed)
        ks = jax.random.split(key, 6)
        s = 1.0 / np.sqrt(IN)
        return {'x': jax.random.normal(ks[0], (N, IN), dtype=jnp.float32), 'edge_index': jax.random.randint(ks[1], (2, E), 0, N, dtype=jnp.int64), 'W_l': jax.random.normal(ks[2], (H * C, IN), dtype=jnp.float32) * s, 'b_l': jnp.zeros((H * C,), jnp.float32), 'W_r': jax.random.normal(ks[3], (H * C, IN), dtype=jnp.float32) * s, 'b_r': jnp.zeros((H * C,), jnp.float32), 'att': jax.random.normal(ks[4], (H, C), dtype=jnp.float32) * s, 'bias': jnp.zeros((H * C,), jnp.float32)}
    _L1_gnn_all = _L1_gnn_setup()
    _L1_gnn_in = {k: v for k, v in _L1_gnn_all.items() if k in ('W_l', 'b_l', 'W_r', 'b_r', 'att', 'bias')}
    del _L1_gnn_all
    return {'x': x, 'src': src, 'dst': dst, 'edge_attr_128': edge_attr_128, 'L0_gnn_msg_W1': _L0_gnn_in['msg_W1'], 'L0_gnn_msg_b1': _L0_gnn_in['msg_b1'], 'L0_gnn_msg_W2': _L0_gnn_in['msg_W2'], 'L0_gnn_msg_b2': _L0_gnn_in['msg_b2'], 'L0_gnn_upd_W1': _L0_gnn_in['upd_W1'], 'L0_gnn_upd_b1': _L0_gnn_in['upd_b1'], 'L0_gnn_upd_W2': _L0_gnn_in['upd_W2'], 'L0_gnn_upd_b2': _L0_gnn_in['upd_b2'], 'L0_gnn_ln_gamma': _L0_gnn_in['ln_gamma'], 'L0_gnn_ln_beta': _L0_gnn_in['ln_beta'], 'L1_gnn_W_l': _L1_gnn_in['W_l'], 'L1_gnn_b_l': _L1_gnn_in['b_l'], 'L1_gnn_W_r': _L1_gnn_in['W_r'], 'L1_gnn_b_r': _L1_gnn_in['b_r'], 'L1_gnn_att': _L1_gnn_in['att'], 'L1_gnn_bias': _L1_gnn_in['bias']}

def reference(x, src, dst, edge_attr_128, L0_gnn_msg_W1, L0_gnn_msg_b1, L0_gnn_msg_W2, L0_gnn_msg_b2, L0_gnn_upd_W1, L0_gnn_upd_b1, L0_gnn_upd_W2, L0_gnn_upd_b2, L0_gnn_ln_gamma, L0_gnn_ln_beta, L1_gnn_W_l, L1_gnn_b_l, L1_gnn_W_r, L1_gnn_b_r, L1_gnn_att, L1_gnn_bias):
    import jax
    import jax.numpy as jnp

    def _L0_gnn_ref(x, edge_index, edge_attr, msg_W1, msg_b1, msg_W2, msg_b2, upd_W1, upd_b1, upd_W2, upd_b2, ln_gamma, ln_beta):
        import jax, jax.numpy as jnp
        import numpy as np
        N_NODES = 6250
        N_EDGES = 80000
        HID = 128
        LN_EPS = 1e-05

        def _layer_norm(h, gamma, beta):
            mu = jnp.mean(h, axis=-1, keepdims=True)
            var = jnp.mean(jnp.square(h - mu), axis=-1, keepdims=True)
            return (h - mu) * jax.lax.rsqrt(var + LN_EPS) * gamma + beta
        src, dst = (edge_index[0], edge_index[1])
        msg_in = jnp.concatenate([x[src], x[dst], edge_attr], axis=-1)
        h = jax.nn.relu(msg_in @ msg_W1 + msg_b1)
        messages = h @ msg_W2 + msg_b2
        aggregated = jax.ops.segment_sum(messages, dst, num_segments=x.shape[0])
        upd_in = jnp.concatenate([x, aggregated], axis=-1)
        u = jax.nn.relu(upd_in @ upd_W1 + upd_b1)
        updated = u @ upd_W2 + upd_b2
        return _layer_norm(x + updated, ln_gamma, ln_beta)

    def _L1_gnn_ref(x, edge_index, W_l, b_l, W_r, b_r, att, bias):
        import jax, jax.numpy as jnp
        import numpy as np
        N = 6250
        E = 75000
        H = 4
        C = 32
        IN = 128
        NEG_SLOPE = 0.2
        n = x.shape[0]
        loops = jnp.arange(n, dtype=edge_index.dtype)
        src = jnp.concatenate([edge_index[0], loops])
        dst = jnp.concatenate([edge_index[1], loops])
        x_l = (x @ W_l.T + b_l).reshape(n, H, C)
        x_r = (x @ W_r.T + b_r).reshape(n, H, C)
        z = jax.nn.leaky_relu(x_l[src] + x_r[dst], NEG_SLOPE)
        e = jnp.einsum('ehc,hc->eh', z, att)
        m = jax.ops.segment_max(e, dst, num_segments=n)
        e = jnp.exp(e - m[dst])
        denom = jax.ops.segment_sum(e, dst, num_segments=n)
        alpha = e / (denom[dst] + 1e-16)
        out = jax.ops.segment_sum(alpha[:, :, None] * x_l[src], dst, num_segments=n)
        out = out.reshape(n, H * C) + bias
        return jax.nn.elu(out)
    edge_index = jnp.stack([src, dst])
    h = jnp.maximum(_layernorm(x, axis=-1), 0.0)
    x = x + _L0_gnn_ref(h, edge_index, edge_attr_128, L0_gnn_msg_W1, L0_gnn_msg_b1, L0_gnn_msg_W2, L0_gnn_msg_b2, L0_gnn_upd_W1, L0_gnn_upd_b1, L0_gnn_upd_W2, L0_gnn_upd_b2, L0_gnn_ln_gamma, L0_gnn_ln_beta)
    h = jnp.maximum(_layernorm(x, axis=-1), 0.0)
    x = x + _L1_gnn_ref(h, edge_index, L1_gnn_W_l, L1_gnn_b_l, L1_gnn_W_r, L1_gnn_b_r, L1_gnn_att, L1_gnn_bias)
    return x

_drawn_inputs = setup_inputs


def setup_inputs(seed=0):
    import zlib

    import numpy as np

    out = dict(_drawn_inputs(seed))
    spreads = {'L0_gnn_msg_b1': (0.0, 0.1),
     'L0_gnn_msg_b2': (0.0, 0.1),
     'L0_gnn_upd_b1': (0.0, 0.8),
     'L0_gnn_upd_b2': (0.0, 0.741),
     'L0_gnn_ln_gamma': (1.0, 0.2),
     'L0_gnn_ln_beta': (0.0, 0.1),
     'L1_gnn_b_l': (0.0, 0.1),
     'L1_gnn_b_r': (0.0, 0.8),
     'L1_gnn_bias': (0.0, 0.1)}
    factors = {'L1_gnn_W_r': 8.0, 'L1_gnn_att': 4.6}
    for name, (base, spread) in spreads.items():
        noise = np.random.default_rng([zlib.crc32(name.encode()), seed]).standard_normal(out[name].shape)
        drawn = base * np.exp(spread * noise) if base else spread * noise
        out[name] = jnp.asarray(drawn.astype(out[name].dtype))
    for name, factor in factors.items():
        out[name] = (out[name] * factor).astype(out[name].dtype)
    return out
```

```python
from contextlib import ExitStack

import concourse.bass as bass
from concourse import mybir

F32 = mybir.dt.float32
BF16 = mybir.dt.bfloat16
I32 = mybir.dt.int32
I16 = mybir.dt.int16
ALU = mybir.AluOpType
ACT = mybir.ActivationFunctionType

P = 128
J = 4
EG = P * J
W = 32
H = 4
U = 8
NTB = 7
HALF = NTB * P // 2
BIG = 1.0e30
HEAD_STEP = 16384.0
SENTINEL = 20000
LN_EPS = 1e-5
SLOPE = 0.2
GATES = {}


def after(eng, sem, count):
    if isinstance(count, int) and count <= 0:
        return
    eng.wait_ge(sem, count)


def hold(eng, sem, count):
    if isinstance(count, int) and count <= 0:
        return
    eng.wait_ge(sem, count)
    if not isinstance(count, int):
        eng.sem_inc(GATES[str(eng.engine)], 1)


def before(rnd, slot, k, tail):
    if tail and slot >= k:
        return None
    slot -= k
    while slot < 0:
        slot += U
        rnd = rnd - 1
    if isinstance(rnd, int) and rnd < 0:
        return None
    return rnd, slot


def rounds(eng, n_rounds, body, tail):
    body(0, range(U), 0)
    with eng.Fori(1, n_rounds) as rnd:
        body(rnd, range(U), 0)
    body(n_rounds, range(tail), 1)


class Kit:
    pass


def gnn_program(nc, t):
    N = t["x"].shape[0]
    E = t["src"].shape[0]
    NT = -(-N // P)
    NI = -(-NT // NTB)
    NT = NI * NTB
    NP = NT * P + W
    NW = NP // W
    NR = -(-E // (EG * U))
    G = NR * U
    NBLK = -(-G // P)
    while G % NBLK:
        NBLK += 1
    GB = G // NBLK
    LAST = N - (N // P) * P
    assert N < SENTINEL and SENTINEL < 2 ** 15 and GB <= P and GB * J <= 512
    k = Kit()
    k.N, k.E, k.NT, k.NI, k.NP, k.NW = N, E, NT, NI, NP, NW
    k.NR, k.G, k.NBLK, k.GB, k.LAST = NR, G, NBLK, GB, LAST

    with ExitStack() as ctx:
        def sb(name, shape, dt):
            return ctx.enter_context(nc.sbuf_tensor(name, shape, dt))

        def sem(name):
            return ctx.enter_context(nc.semaphore(name))

        def dram(name, shape, dt):
            return nc.dram_tensor(name, shape, dt).ap()

        k.tab_a = dram("tab_a", [NP, P], F32)
        k.tab_b = dram("tab_b", [NP, P], F32)
        k.tab_b3 = dram("tab_b3", [3, NP, P], BF16)
        k.tab_l = dram("tab_l", [NP, P], F32)
        k.tab_r = dram("tab_r", [NP, P], F32)
        k.tab_r3 = dram("tab_r3", [3, NP, P], BF16)
        k.tab_es = dram("tab_es", [H, NP], F32)
        k.dst_rows = dram("dst_rows", [G, EG], I16)

        k.X = sb("X", [P, NT, P], F32)
        k.HT = sb("HT", [P, NT * P], F32)
        k.acc = sb("acc", [P, 2, NP], F32)
        k.src_t = sb("src_t", [P, G + U, J], F32)
        k.dst_t = sb("dst_t", [P, G + U, J], F32)
        k.base = sb("base", [P, G], F32)
        k.win_id = sb("win_id", [P, G], F32)
        k.shift_id = sb("shift_id", [P, G], F32)
        k.gen_base = sb("gen_base", [P, NW], F32)
        k.gen_win_id = sb("gen_win_id", [P, NW], F32)
        k.base_i = sb("base_i", [1, G], I32)
        k.flag_i = sb("flag_i", [1, 1], I32)

        k.ident = sb("ident", [P, P], F32)
        k.ones = sb("ones", [P, P], F32)
        k.zrow = sb("zrow", [W, P], F32)
        k.pm = sb("pm", [P, 1], F32)
        k.ph = sb("ph", [P, 1], F32)
        k.iota_w = sb("iota_w", [P, W], F32)
        k.iota_h = sb("iota_h", [P, H], F32)
        k.iota_c = sb("iota_c", [P, P], F32)
        k.iota_q = sb("iota_q", [P, P], F32)
        k.same_head = sb("same_head", [P, P], F32)
        k.head4 = sb("head4", [P, H], F32)
        k.diag_w = sb("diag_w", [P, W], F32)
        k.eps = sb("eps", [P, 1], F32)
        k.w1 = sb("w1", [P, 3, P], F32)
        k.w1ab = sb("w1ab", [P, 2, P], F32)
        k.w2 = sb("w2", [P, P], F32)
        k.u1 = sb("u1", [P, 2, P], F32)
        k.u2 = sb("u2", [P, P], F32)
        k.wl = sb("wl", [P, P], F32)
        k.wr = sb("wr", [P, P], F32)
        k.wlr = sb("wlr", [P, 2, P], F32)
        k.b2 = sb("b2", [1, P], F32)
        k.ub2 = sb("ub2", [P, 1], F32)
        k.b1_bc = sb("b1_bc", [P, P], F32)
        k.gamma_bc = sb("gamma_bc", [P, P], F32)
        k.beta_bc = sb("beta_bc", [P, P], F32)
        k.blr_bc = sb("blr_bc", [P, 2, P], F32)
        k.ub1 = sb("ub1", [P, 1], F32)
        k.bl = sb("bl", [P, 1], F32)
        k.br = sb("br", [P, 1], F32)
        k.blr = sb("blr", [P, 1], F32)
        k.bias = sb("bias", [P, 1], F32)
        k.att = sb("att", [P, 1], F32)
        k.att4 = sb("att4", [P, H], F32)
        k.att_w = sb("att_w", [P, P], F32)

        k.bank = [ctx.enter_context(nc.psum_tensor(f"bank{i}", [P, 512], F32)) for i in range(8)]
        for eng in (nc.tensor, nc.vector, nc.scalar, nc.gpsimd, nc.sync):
            GATES[str(eng.engine)] = sem("gate_" + str(eng.engine).split(".")[-1].lower())
        setup(nc, t, k)
        nodes_first(nc, t, k)
        edges_mlp(nc, t, k)
        nodes_middle(nc, t, k)
        edges_attention(nc, t, k)
        nodes_last(nc, t, k)


class Sems:

    def __init__(self, nc, ctx):
        self.nc, self.ctx, self.all = nc, ctx, []

    def one(self, name):
        self.all.append(self.ctx.enter_context(self.nc.semaphore(name)))
        return self.all[-1]

    def named(self, names, tag=""):
        return {n: self.one(tag + n) for n in names.split()}

    def clear(self):
        with self.nc.Block() as block:
            @block.sync
            def _(sp):
                for one in self.all:
                    sp.sem_clear(one)


def setup(nc, t, k):
    E, G, GB, NBLK = k.E, k.G, k.GB, k.NBLK
    full, rest = E // EG, E % EG
    with ExitStack() as ctx:
        sems = Sems(nc, ctx)
        s = sems.named("s_pad s_rows s_w s_zero s_iota s_f s_tp s_tcopy s_perm s_permout s_chain s_basep s_wt "
                             "s_wtc s_cnt s_flagp s_zt")
        rows_i = ctx.enter_context(nc.sbuf_tensor("rows_i", [GB, 2, NBLK, EG], I32))
        rows_f = ctx.enter_context(nc.sbuf_tensor("rows_f", [GB, 2, NBLK, EG], F32))
        perm = ctx.enter_context(nc.sbuf_tensor("perm", [GB, NBLK, EG], I16))
        rel = ctx.enter_context(nc.sbuf_tensor("rel", [P, G, J], F32))
        hit = ctx.enter_context(nc.sbuf_tensor("hit", [P, G, J], F32))
        cnt = ctx.enter_context(nc.sbuf_tensor("cnt", [P, 4], F32))
        with nc.Block() as block:

            @block.sync
            def _(sp):
                sp.wait_ge(s["s_pad"], 2)
                n = 0
                for v, name in enumerate(("src", "dst")):
                    for b in range(NBLK):
                        r = min(max(full - b * GB, 0), GB)
                        if r:
                            sp.dma_start(rows_i[0:r, v, b, :],
                                         t[name][b * GB * EG:(b * GB + r) * EG].rearrange("(g e) -> g e", e=EG)
                                         ).then_inc(s["s_rows"], 16)
                            n += 1
                    if rest:
                        b, r = full // GB, full % GB
                        sp.dma_start(rows_i[r:r + 1, v, b, 0:rest],
                                     t[name][full * EG:E].rearrange("(a e) -> a e", a=1)).then_inc(s["s_rows"], 16)
                        n += 1
                k.n_rows = n
                sp.wait_ge(s["s_zt"], 1)
                nt = k.N // P
                for i in range(0, nt, NTB):
                    m = min(nt, i + NTB)
                    sp.dma_start(k.X[:, i:m, :], t["x"][i * P:m * P, :].rearrange("(t p) d -> p t d", p=P)
                                 ).then_inc(s["s_w"], 16)
                if k.LAST:
                    sp.dma_start(k.X[0:k.LAST, nt, :], t["x"][nt * P:k.N, :]).then_inc(s["s_w"], 16)
                sp.wait_ge(s["s_zero"], 1)
                z16 = k.zrow[:].bitcast(BF16)[:, 0:P]
                top = k.NP - W
                for tab in (k.tab_b3, k.tab_r3):
                    for part in range(3):
                        sp.dma_start(tab[part, top:k.NP, :], z16).then_inc(s["s_w"], 16)
                for tab in (k.tab_b, k.tab_r, k.tab_a, k.tab_l):
                    sp.dma_start(tab[top:k.NP, :], k.zrow[:]).then_inc(s["s_w"], 16)
                sp.dma_start(k.tab_es[:, top:k.NP], k.zrow[0:H, 0:W]).then_inc(s["s_w"], 16)
                sp.wait_ge(s["s_perm"], 1)
                sp.dma_start(k.dst_rows.rearrange("(b g) e -> g b e", g=GB), perm[:]).then_inc(s["s_permout"], 16)
                sp.wait_ge(s["s_permout"], 16)
                sp.wait_ge(s["s_w"], 16 * (-(-nt // NTB) + bool(k.LAST) + 11))

            @block.scalar
            def _(act):
                def col(name):
                    return t[name].rearrange("(p a) -> p a", a=1)

                def row(name):
                    return t[name].rearrange("(a d) -> a d", a=1)

                loads = [
                    (k.w1[:], t["L0_gnn_msg_W1"].rearrange("(c p) d -> p c d", p=P)),
                    (k.w2[:], t["L0_gnn_msg_W2"]),
                    (k.u1[:], t["L0_gnn_upd_W1"].rearrange("(c p) d -> p c d", p=P)),
                    (k.u2[:], t["L0_gnn_upd_W2"]),
                    (k.wl[:], t["L1_gnn_W_l"]), (k.wr[:], t["L1_gnn_W_r"]),
                    (k.b2[:], row("L0_gnn_msg_b2")), (k.ub2[:], col("L0_gnn_upd_b2")),
                    (k.b1_bc[:], row("L0_gnn_msg_b1").to_broadcast([P, P])),
                    (k.gamma_bc[:], row("L0_gnn_ln_gamma").to_broadcast([P, P])),
                    (k.beta_bc[:], row("L0_gnn_ln_beta").to_broadcast([P, P])),
                    (k.blr_bc[:, 0, :], row("L1_gnn_b_l").to_broadcast([P, P])),
                    (k.blr_bc[:, 1, :], row("L1_gnn_b_r").to_broadcast([P, P])),
                    (k.ub1[:], col("L0_gnn_upd_b1")), (k.bl[:], col("L1_gnn_b_l")), (k.br[:], col("L1_gnn_b_r")),
                    (k.bias[:], col("L1_gnn_bias")),
                    (k.att[:], t["L1_gnn_att"].rearrange("h (c a) -> (h c) a", a=1)),
                ]
                k.n_w = len(loads)
                for dst, src in loads:
                    act.dma_start(dst, src).then_inc(s["s_wt"], 16)
                act.wait_ge(s["s_wt"], 16 * len(loads))

            @block.gpsimd
            def _(pool):
                pool.memset(rows_i[:, 0], 0).then_inc(s["s_pad"], 1)
                pool.memset(rows_i[:, 1], SENTINEL).then_inc(s["s_pad"], 1)
                pool.memset(k.zrow[:], 0.0).then_inc(s["s_zero"], 1)
                pool.memset(k.ident[:], 0.0).then_inc(s["s_iota"], 1)
                pool.wait_ge(s["s_iota"], 1)
                pool.affine_select(out=k.ident[:], in_=k.ident[:], compare_op=ALU.not_equal, fill=1.0, base=0,
                                   pattern=[[-1, P]], channel_multiplier=1)
                pool.memset(k.ones[:], 1.0)
                pool.memset(k.eps[:], LN_EPS)

                def iota(out, pattern, cm, b=0):
                    return pool.iota(out, pattern=pattern, base=b, channel_multiplier=cm,
                                     allow_small_or_imprecise_dtypes=True)

                iota(k.iota_w[:], [[1, W]], 0)
                iota(k.iota_h[:], [[1, H]], 0)
                iota(k.iota_c[:], [[int(HEAD_STEP), H], [1, W]], 0)
                iota(k.iota_q[:], [[1, H], [0, W]], 0)
                iota(k.gen_base[:], [[W, k.NW]], 0)
                iota(k.pm[:], [[0, 1]], 1).then_inc(s["s_iota"], 1)

            @block.tensor
            def _(pe):
                pe.wait_ge(s["s_iota"], 2)
                for v in range(2):
                    pe.wait_ge(s["s_f"], v + 1)
                    for b in range(NBLK):
                        n = v * NBLK + b
                        after(pe, s["s_tcopy"], n - 1)
                        r = rows_f[:, v, b, :].rearrange("g (p j) -> g j p", j=J)
                        for j in range(J):
                            last = pe.transpose(k.bank[n % 2][:, j * GB:(j + 1) * GB], r[:, j, :],
                                                k.ident[0:GB, 0:GB])
                        last.then_inc(s["s_tp"], 1)
                pe.wait_ge(s["s_wt"], 16 * 18)
                pe.transpose(k.bank[3][:, 0:P], k.wl[:], k.ident[:])
                pe.transpose(k.bank[3][:, P:2 * P], k.wr[:], k.ident[:]).then_inc(s["s_wtc"], 1)
                pe.wait_ge(s["s_tcopy"], 2 * NBLK)
                pe.matmul(k.bank[2][:, 0:G], lhsT=k.ones[0:1, :], rhs=k.dst_t[0:1, 0:G, 0], start=True, stop=True
                          ).then_inc(s["s_basep"], 1)
                pe.wait_ge(s["s_cnt"], 1)
                pe.matmul(k.bank[4][:, 0:1], lhsT=k.ones[:], rhs=cnt[:, 2:3], start=True, stop=True
                          ).then_inc(s["s_flagp"], 1)

            @block.vector
            def _(dve):
                links = [0]

                def link(ins):
                    links[0] += 1
                    ins.then_inc(s["s_chain"], 1)
                    dve.wait_ge(s["s_chain"], links[0])

                dve.memset(k.X[:, k.N // P:, :], 0.0).then_inc(s["s_zt"], 1)
                dve.memset(k.src_t[:, G:, :], 0.0)
                dve.memset(k.dst_t[:, G:, :], 0.0)
                dve.memset(k.acc[:], 0.0)
                dve.wait_ge(s["s_rows"], 16 * 2 * (sum(1 for b in range(NBLK) if full > b * GB) + bool(rest)))
                for v in range(2):
                    dve.tensor_copy(rows_f[:, v], rows_i[:, v]).then_inc(s["s_f"], 1)
                for b in range(NBLK):
                    last = dve.tensor_copy(perm[:, b, :].rearrange("g (j p) -> g j p", j=J),
                                           rows_i[:, 1, b, :].rearrange("g (p j) -> g j p", j=J))
                last.then_inc(s["s_perm"], 1)
                for v, table in enumerate((k.src_t, k.dst_t)):
                    for b in range(NBLK):
                        n = v * NBLK + b
                        dve.wait_ge(s["s_tp"], n + 1)
                        dve.tensor_copy(table[:, b * GB:(b + 1) * GB, :],
                                        k.bank[n % 2][:, 0:J * GB].rearrange("p (j g) -> p g j", j=J)
                                        ).then_inc(s["s_tcopy"], 1)
                dve.wait_ge(s["s_iota"], 2)
                link(dve.tensor_scalar(k.ph[:], k.pm[:], float(W), None, ALU.is_ge))
                for h in range(2, H):
                    link(dve.scalar_tensor_tensor(out=k.ph[:], in0=k.pm[:], scalar=float(h * W), in1=k.ph[:],
                                                  op0=ALU.is_ge, op1=ALU.add))
                link(dve.scalar_tensor_tensor(out=k.pm[:], in0=k.ph[:], scalar=-float(W), in1=k.pm[:],
                                              op0=ALU.mult, op1=ALU.add))
                dve.tensor_scalar(k.gen_win_id[:], k.gen_base[:], k.pm[:, 0:1], None, ALU.add)
                dve.tensor_scalar(k.same_head[:], k.iota_q[:], k.ph[:, 0:1], None, ALU.is_equal)
                dve.tensor_scalar(k.diag_w[:], k.iota_w[:], k.pm[:, 0:1], None, ALU.is_equal)
                link(dve.tensor_scalar(k.head4[:], k.iota_h[:], k.ph[:, 0:1], None, ALU.is_equal))
                dve.wait_ge(s["s_wt"], 16 * 18)
                dve.tensor_scalar(k.att4[:], k.head4[:], k.att[:, 0:1], None, ALU.mult)
                dve.tensor_scalar(k.att_w[:], k.same_head[:], k.att[:, 0:1], None, ALU.mult)
                dve.tensor_tensor(k.blr[:], k.bl[:], k.br[:], ALU.add)
                dve.tensor_copy(k.w1ab[:], k.w1[:, 0:2, :])
                dve.wait_ge(s["s_wtc"], 1)
                dve.tensor_copy(k.wlr[:].rearrange("p a d -> p (a d)"), k.bank[3][:, 0:2 * P])
                dve.wait_ge(s["s_basep"], 1)
                link(dve.tensor_scalar(k.base[:], k.bank[2][:, 0:G], float(k.NP - W), None, ALU.min))
                dve.tensor_copy(k.base_i[:], k.base[0:1, :])
                dve.tensor_scalar(k.win_id[:], k.base[:], k.pm[:, 0:1], None, ALU.add)
                link(dve.memset(k.shift_id[:, 0:1], -1.0e6))
                link(dve.tensor_tensor(k.shift_id[:, 1:G], k.base[:, 0:G - 1], k.base[:, 1:G], ALU.subtract))
                link(dve.tensor_scalar(cnt[:, 3:4], k.ph[:], HEAD_STEP, None, ALU.mult))
                link(dve.tensor_scalar(k.shift_id[:, 1:G], k.shift_id[:, 1:G], k.pm[:, 0:1], cnt[:, 3:4],
                                       ALU.add, ALU.add))
                link(dve.tensor_tensor(rel[:], k.dst_t[:, 0:G, :],
                                       k.base[:].unsqueeze(2).to_broadcast([P, G, J]), ALU.subtract))
                link(dve.tensor_scalar(hit[:], rel[:], 0.0, None, ALU.is_ge))
                link(dve.scalar_tensor_tensor(out=rel[:], in0=rel[:], scalar=float(W), in1=hit[:],
                                              op0=ALU.is_lt, op1=ALU.mult))
                link(dve.tensor_reduce(cnt[:, 0:1], rel[:], mybir.AxisListType.XY, ALU.add))
                link(dve.tensor_tensor(hit[:].rearrange("p g j -> p (g j)")[:, 0:G - 1], k.base[:, 1:G],
                                       k.base[:, 0:G - 1], ALU.is_ge))
                link(dve.tensor_reduce(cnt[:, 1:2], hit[:].rearrange("p g j -> p (g j)")[:, 0:G - 1],
                                       mybir.AxisListType.X, ALU.add))
                dve.tensor_tensor(cnt[:, 2:3], cnt[:, 0:1], cnt[:, 1:2], ALU.add).then_inc(s["s_cnt"], 1)
                dve.wait_ge(s["s_flagp"], 1)
                link(dve.tensor_scalar(k.flag_i[:], k.bank[4][0:1, 0:1], float(E + P * (G - 1)), None,
                                       ALU.is_equal))
        sems.clear()


def store_tables(eng, s, k, first_sem, rows, plain, split):
    for (tab, buf) in plain:
        eng.dma_start(tab[bass.ds(rows, NTB * P), :].rearrange("(t p) d -> p t d", p=P), buf).then_inc(first_sem, 16)
    for (tab, buf) in split:
        for part in range(3):
            eng.dma_start(tab[part, bass.ds(rows, NTB * P), :].rearrange("(t p) d -> p t d", p=P), buf[part]
                          ).then_inc(first_sem, 16)


def nodes_first(nc, t, k):
    N2 = NTB * P
    with ExitStack() as ctx:
        sems = Sems(nc, ctx)
        s = sems.named("a_st a_var a_sd a_rs a_nm a_h a_tp a_ht a_ab a_acp a_b a_hi a_r a_mid a_lo a_out a_kept")
        st = ctx.enter_context(nc.sbuf_tensor("st", [P, NTB, 6], F32))
        mv = ctx.enter_context(nc.sbuf_tensor("mv", [P, NTB, 2], F32))
        sd = ctx.enter_context(nc.sbuf_tensor("sd", [P, NTB], F32))
        rs = ctx.enter_context(nc.sbuf_tensor("rs", [P, NTB], F32))
        nm = ctx.enter_context(nc.sbuf_tensor("nm", [P, NTB], F32))
        hb = ctx.enter_context(nc.sbuf_tensor("hb", [P, NTB, P], F32))
        ht = ctx.enter_context(nc.sbuf_tensor("ht", [P, NTB * P], F32))
        at = ctx.enter_context(nc.sbuf_tensor("at", [P, NTB, P], F32))
        bt = ctx.enter_context(nc.sbuf_tensor("bt", [P, NTB, P], F32))
        r1 = ctx.enter_context(nc.sbuf_tensor("r1", [P, NTB, P], F32))
        b3 = [ctx.enter_context(nc.sbuf_tensor(f"b3{q}", [P, NTB, P], BF16)) for q in range(3)]
        def hp(tile):
            return k.bank[tile // 4][:, (tile % 4) * P:(tile % 4 + 1) * P]

        def ab(tile):
            return k.bank[2 + tile // 2][:, (tile % 2) * 2 * P:(tile % 2 + 1) * 2 * P]

        with nc.Block() as block:

            @block.vector
            def _(dve):
                with dve.Fori(0, k.NI) as i:
                    for q in range(NTB):
                        last = dve.bn_stats(st[:, q, :], k.X[:, bass.ds(i * NTB + q, 1), :])
                    last.then_inc(s["a_st"], 1)
                    hold(dve, s["a_st"], i + 1)
                    for q in range(NTB):
                        last = dve.bn_aggr(mv[:, q, :], st[:, q, :])
                    last.then_inc(s["a_var"], 1)
                    dve.wait_ge(s["a_sd"], i + 1)
                    dve.reciprocal(rs[:], sd[:]).then_inc(s["a_rs"], 1)
                    dve.wait_ge(s["a_rs"], i + 1)
                    dve.scalar_tensor_tensor(out=nm[:], in0=mv[:, :, 0], scalar=-1.0, in1=rs[:], op0=ALU.mult,
                                             op1=ALU.mult).then_inc(s["a_nm"], 1)
                    dve.wait_ge(s["a_acp"], i + 1)
                    for q in range(NTB):
                        last = dve.tensor_tensor(bt[:, q, :], ab(q)[:, P:2 * P], k.b1_bc[:], ALU.add)
                    last.then_inc(s["a_b"], 1)
                    dve.wait_ge(s["a_hi"], i + 1)
                    dve.tensor_tensor(r1[:], bt[:], b3[0][:], ALU.subtract).then_inc(s["a_r"], 1)
                    dve.wait_ge(s["a_mid"], i + 1)
                    dve.tensor_tensor(b3[2][:], r1[:], b3[1][:], ALU.subtract).then_inc(s["a_lo"], 1)
                    dve.wait_ge(s["a_out"], (i + 1) * 16 * 5)

            @block.scalar
            def _(act):
                with act.Fori(0, k.NI) as i:
                    act.wait_ge(s["a_var"], i + 1)
                    act.activation(sd[:], mv[:, :, 1], ACT.Sqrt, bias=k.eps[:, 0:1]).then_inc(s["a_sd"], 1)
                    hold(act, s["a_nm"], i + 1)
                    for q in range(NTB):
                        last = act.activation(hb[:, q, :], k.X[:, bass.ds(i * NTB + q, 1), :], ACT.Relu,
                                              scale=rs[:, q:q + 1], bias=nm[:, q:q + 1])
                    last.then_inc(s["a_h"], 1)
                    act.wait_ge(s["a_tp"], i + 1)
                    act.activation(ht[:, 0:512], k.bank[0][:], ACT.Copy)
                    act.activation(ht[:, 512:N2], k.bank[1][:, 0:N2 - 512], ACT.Copy).then_inc(s["a_ht"], 1)
                    act.wait_ge(s["a_ab"], i + 1)
                    for q in range(NTB):
                        last = act.activation(at[:, q, :], ab(q)[:, 0:P], ACT.Copy)
                    last.then_inc(s["a_acp"], 1)
                    act.wait_ge(s["a_b"], i + 1)
                    act.activation(b3[0][:], bt[:], ACT.Copy).then_inc(s["a_hi"], 1)
                    act.wait_ge(s["a_r"], i + 1)
                    act.activation(b3[1][:], r1[:], ACT.Copy).then_inc(s["a_mid"], 1)
                    act.wait_ge(s["a_kept"], i + 1)
                    act.wait_ge(s["a_out"], (i + 1) * 16 * 5)

            @block.tensor
            def _(pe):
                with pe.Fori(0, k.NI) as i:
                    pe.wait_ge(s["a_h"], i + 1)
                    for q in range(NTB):
                        last = pe.transpose(hp(q), hb[:, q, :], k.ident[:])
                    last.then_inc(s["a_tp"], 1)
                    pe.wait_ge(s["a_ht"], i + 1)
                    for q in range(NTB):
                        last = pe.matmul(ab(q), lhsT=ht[:, q * P:(q + 1) * P], rhs=k.w1ab[:].rearrange("p a d -> p (a d)"), start=True, stop=True)
                    last.then_inc(s["a_ab"], 1)

            @block.gpsimd
            def _(pool):
                with pool.Fori(0, k.NI) as i:
                    hold(pool, s["a_ht"], i + 1)
                    pool.tensor_copy(k.HT[:, bass.ds(i * N2, N2)], ht[:]).then_inc(s["a_kept"], 1)

            @block.sync
            def _(sp):
                with sp.Fori(0, k.NI) as i:
                    sp.wait_ge(s["a_acp"], i + 1)
                    sp.wait_ge(s["a_lo"], i + 1)
                    store_tables(sp, s, k, s["a_out"], i * N2, [(k.tab_a, at[:]), (k.tab_b, bt[:])],
                                 [(k.tab_b3, [b[:] for b in b3])])
                sp.wait_ge(s["a_out"], k.NI * 16 * 5)
        sems.clear()


def edge_slots(ctx, nc, sems, tag):
    def sb(name, shape, dt):
        return ctx.enter_context(nc.sbuf_tensor(f"{tag}_{name}", shape, dt))

    r = Kit()
    r.idx = [sb(f"idx{u}", [P, J], I32) for u in range(U)]
    r.got = [sb(f"got{u}", [P, J, P], F32) for u in range(U)]
    r.row = [sb(f"row{u}", [P, EG], I16) for u in range(U)]
    r.win = [sb(f"win{u}", [3 * W, P], BF16) for u in range(U)]
    r.s_got = [sems.one(f"{tag}_got{u}") for u in range(U)]
    r.s_in = [sems.one(f"{tag}_in{u}") for u in range(U)]
    r.s_idx = sems.one(f"{tag}_idx")
    return r


def is_fast(eng, k):
    return eng.value_load(k.flag_i[0:1, 0:1], min_val=0, max_val=1) != 0


def gather_rounds(pool, k, r, table, s_freed):
    def body(rnd, slots, _):
        for u in slots:
            g = rnd * U + u
            hold(pool, r.s_idx, g + 1)
            hold(pool, s_freed, g + 1 - U)
            for j in range(J):
                pool.indirect_dma_start(out=r.got[u][:, j, :], out_offset=None, in_=table,
                                        in_offset=bass.IndirectOffsetOnAxis(ap=r.idx[u][:, j:j + 1], axis=0)
                                        ).then_inc(r.s_got[u], 16)

    rounds(pool, k.NR, body, 0)


class General:

    def __init__(self, sems, k, tag, names):
        self.k, self.s = k, sems.named(names, tag)
        self.groups = -(-k.E // EG)

    def each_group(self, eng, body):
        if self.groups > 1:
            with eng.Fori(0, self.groups - 1) as g:
                body(g)
        body(self.groups - 1)

    def each_window(self, eng, g, body):
        with eng.Fori(0, self.k.NW) as w:
            body(w, g * self.k.NW + w)


class Chain:

    def __init__(self, eng, sem, size, step):
        self.eng, self.sem, self.size, self.step, self.n = eng, sem, size, step, 0

    def link(self, ins):
        self.n += 1
        assert self.n <= self.size
        ins.then_inc(self.sem, 1)
        hold(self.eng, self.sem, self.step * self.size + self.n)

    def done(self):
        assert self.n == self.size


def general_indices(dve, k, chain, ids, g):
    chain.link(dve.tensor_copy(ids[:, 0, :], k.src_t[:, bass.ds(g, 1), :].rearrange("p a j -> p (a j)")))
    chain.link(dve.tensor_scalar(ids[:, 1, :], k.dst_t[:, bass.ds(g, 1), :].rearrange("p a j -> p (a j)"),
                                 float(k.NP - 1), None, ALU.min))


def general_gathers(pool, ids, got, tables, s_idx, s_got, s_used, g):
    hold(pool, s_idx, 2 * (g + 1))
    for v, table in enumerate(tables):
        for j in range(J):
            pool.indirect_dma_start(out=got[v][:, j, :], out_offset=None, in_=table,
                                    in_offset=bass.IndirectOffsetOnAxis(ap=ids[:, v, j:j + 1], axis=0)
                                    ).then_inc(s_got, 16)
    hold(pool, s_used, g + 1)


def general_hot(dve, k, hot, g, w):
    return dve.scalar_tensor_tensor(
        out=hot[:], in0=k.iota_w[:].unsqueeze(1).to_broadcast([P, J, W]), scalar=k.gen_base[:, bass.ds(w, 1)],
        in1=k.dst_t[:, bass.ds(g, 1), :].rearrange("p a j -> p (a j)").unsqueeze(2).to_broadcast([P, J, W]),
        op0=ALU.add, op1=ALU.is_equal)


def edges_mlp(nc, t, k):
    G, NR = k.G, k.NR
    ea = t["edge_attr_128"]
    full, rest = k.E // EG, k.E % EG
    with ExitStack() as ctx:
        sems = Sems(nc, ctx)
        r = edge_slots(ctx, nc, sems, "m")
        s = sems.named("m_masks m_attrp m_attr m_hp m_sum m_h m_aggp m_agg m_zero m_tmp "
                             "m_done")

        def sb(name, shape, dt):
            return ctx.enter_context(nc.sbuf_tensor(name, shape, dt))

        attr = [sb(f"m_attr_in{u}", [P, J, P], F32) for u in range(U)]
        attr_t = [sb(f"m_attr_t{q}", [P, EG], F32) for q in range(2)]
        hot_t = [sb(f"m_hot_t{q}", [P, EG], BF16) for q in range(2)]
        hot = [sb(f"m_hot{q}", [P, J, W], F32) for q in range(4)]
        pre = [sb(f"m_pre{q}", [P, EG], F32) for q in range(2)]
        hid = [sb(f"m_hid{q}", [P, EG], F32) for q in range(2)]
        p_attr, p_hid, p_agg = k.bank[0:2], k.bank[2:4], k.bank[4:6]

        def load(sp, g, u):
            if isinstance(g, int) and g >= full:
                if g == full and rest:
                    sp.dma_start(attr[u][0:rest // J, :, :],
                                 ea[g * EG:k.E, :].rearrange("(p j) d -> p j d", j=J)).then_inc(r.s_in[u], 16)
                else:
                    sp.dma_start(attr[u][0:P // 2, :, :], ea[0:P // 2 * J, :].rearrange("(p j) d -> p j d", j=J)
                                 ).then_inc(r.s_in[u], 16)
            else:
                sp.dma_start(attr[u][:], ea[bass.ds(g * EG, EG), :].rearrange("(p j) d -> p j d", j=J)
                             ).then_inc(r.s_in[u], 16)
            sp.dma_start(r.row[u][:], k.dst_rows[bass.ds(g, 1), :].to_broadcast([P, EG])).then_inc(r.s_in[u], 16)
            n0 = sp.value_load(k.base_i[0:1, bass.ds(g, 1)], min_val=0, max_val=k.NP - W)
            for part in range(3):
                sp.dma_start(r.win[u][part * W:(part + 1) * W, :], k.tab_b3[part, bass.ds(n0, W), :]
                             ).then_inc(r.s_in[u], 16)

        n_in = 16 * 5

        gen = General(sems, k, "x", "in idx got attrp attr hp chain sum h hot aggp acc")
        x = gen.s
        ids = sb("x_ids", [P, 2, J], I32)
        got = [r.got[0], r.got[1]]
        pre_b, pre_a, hid_g, hot_g = pre[0], pre[1], hid[0], hot[0]

        def general_sync(sp):
            def group(g):
                if isinstance(g, int) and rest:
                    sp.dma_start(attr[0][0:rest // J, :, :], ea[g * EG:k.E, :].rearrange("(p j) d -> p j d", j=J)
                                 ).then_inc(x["in"], 16)
                else:
                    sp.dma_start(attr[0][:], ea[bass.ds(g * EG, EG), :].rearrange("(p j) d -> p j d", j=J)
                                 ).then_inc(x["in"], 16)
                hold(sp, x["attrp"], g + 1)

            gen.each_group(sp, group)

        def general_gpsimd(pool):
            gen.each_group(pool, lambda g: general_gathers(pool, ids, got, (k.tab_a, k.tab_b), x["idx"], x["got"],
                                                           x["sum"], g))

        def general_tensor(pe):
            def group(g):
                hold(pe, x["in"], 16 * (g + 1))
                for j in range(J):
                    last = pe.transpose(p_attr[0][:, j * P:(j + 1) * P], attr[0][:, j, :], k.ident[:])
                last.then_inc(x["attrp"], 1)
                hold(pe, x["attr"], g + 1)
                for j in range(J):
                    e = slice(j * P, (j + 1) * P)
                    last = pe.matmul(p_hid[0][:, e], lhsT=attr_t[0][:, e], rhs=k.w1[:, 2, :], start=True, stop=True)
                last.then_inc(x["hp"], 1)
                hold(pe, x["h"], g + 1)

                def window(w, step):
                    hold(pe, x["hot"], step + 1)
                    for c in range(2):
                        for j in range(J):
                            lhs = k.ones[:] if c else hid_g[:, j * P:(j + 1) * P]
                            last = pe.matmul(p_agg[0][:, c * W:(c + 1) * W], lhsT=lhs, rhs=hot_g[:, j, :],
                                             start=(j == 0), stop=(j == J - 1))
                    last.then_inc(x["aggp"], 1)
                    hold(pe, x["acc"], step + 1)

                gen.each_window(pe, g, window)

            gen.each_group(pe, group)

        def general_scalar(act):
            def group(g):
                hold(act, x["attrp"], g + 1)
                act.activation(attr_t[0][:], p_attr[0][:], ACT.Copy).then_inc(x["attr"], 1)
                hold(act, x["sum"], g + 1)
                act.activation(hid_g[:], pre_b[:], ACT.Relu).then_inc(x["h"], 1)

            gen.each_group(act, group)

        def general_vector(dve):
            def group(g):
                general_indices(dve, k, Chain(dve, x["idx"], 2, g), ids, g)
                hold(dve, x["hp"], g + 1)
                hold(dve, x["got"], 16 * 2 * J * (g + 1))
                Chain(dve, x["chain"], 1, g).link(dve.tensor_tensor(
                    pre_a[:], p_hid[0][:], got[0][:].rearrange("p j d -> p (j d)"), ALU.add))
                dve.tensor_tensor(pre_b[:], pre_a[:], got[1][:].rearrange("p j d -> p (j d)"), ALU.add
                                  ).then_inc(x["sum"], 1)

                def window(w, step):
                    general_hot(dve, k, hot_g, g, w).then_inc(x["hot"], 1)
                    hold(dve, x["aggp"], step + 1)
                    cols = k.acc[:, :, bass.ds(w * W, W)]
                    dve.tensor_tensor(cols, cols, p_agg[0][:, 0:2 * W].rearrange("p (c w) -> p c w", c=2), ALU.add
                                      ).then_inc(x["acc"], 1)
                    hold(dve, x["acc"], step + 1)

                gen.each_window(dve, g, window)

            gen.each_group(dve, group)

        with nc.Block() as block:

            @block.sync
            def _(sp):
                with sp.If(is_fast(sp, k)):
                    for u in range(U):
                        load(sp, u, u)
                    with sp.Fori(1, NR - 1) as rnd:
                        for u in range(U):
                            g = rnd * U + u
                            hold(sp, s["m_hp"], g + 1 - U)
                            load(sp, g, u)
                    for u in range(U):
                        g = (NR - 1) * U + u
                        hold(sp, s["m_hp"], g + 1 - U)
                        load(sp, g, u)
                with sp.Else():
                    general_sync(sp)

            @block.gpsimd
            def _(pool):
                with pool.If(is_fast(pool, k)):
                    gather_rounds(pool, k, r, k.tab_a, s["m_sum"])
                with pool.Else():
                    general_gpsimd(pool)

            @block.tensor
            def _(pe):
                with pe.If(is_fast(pe, k)):
                    def body(rnd, slots, tail):
                        for u in slots:
                            if not tail:
                                g = rnd * U + u
                                hold(pe, r.s_in[u], n_in * (rnd + 1))
                                hold(pe, s["m_attr"], g - 1)
                                for j in range(J):
                                    last = pe.transpose(p_attr[u % 2][:, j * P:(j + 1) * P], attr[u][:, j, :], k.ident[:])
                                last.then_inc(s["m_attrp"], 1)
                            if at := before(rnd, u, 1, tail):
                                g, q = at[0] * U + at[1], at[1]
                                hold(pe, s["m_masks"], g + 1)
                                hold(pe, s["m_attr"], g + 1)
                                hold(pe, s["m_sum"], g - 1)
                                for j in range(J):
                                    e = slice(j * P, (j + 1) * P)
                                    pe.matmul(p_hid[q % 2][:, e], lhsT=attr_t[q % 2][:, e], rhs=k.w1[:, 2, :],
                                              start=True, stop=False)
                                    last = pe.matmul(p_hid[q % 2][:, e], lhsT=hot_t[q % 2][0:3 * W, e], rhs=r.win[q][:],
                                                     start=False, stop=True)
                                last.then_inc(s["m_hp"], 1)
                            if at := before(rnd, u, 2, tail):
                                g, q = at[0] * U + at[1], at[1]
                                hold(pe, s["m_h"], g + 1)
                                hold(pe, s["m_agg"], g - 1)
                                for c, left in enumerate((hid[q % 2], None)):
                                    for j in range(J):
                                        lhs = k.ones[:] if left is None else left[:, j * P:(j + 1) * P]
                                        last = pe.matmul(p_agg[q % 2][:, c * W:(c + 1) * W], lhsT=lhs,
                                                         rhs=hot[q % 4][:, j, :], start=(j == 0), stop=(j == J - 1))
                                last.then_inc(s["m_aggp"], 1)

                    rounds(pe, NR, body, 2)
                with pe.Else():
                    general_tensor(pe)

            @block.scalar
            def _(act):
                with act.If(is_fast(act, k)):
                    def body(rnd, slots, tail):
                        for u in slots:
                            if not tail:
                                g = rnd * U + u
                                after(act, s["m_attrp"], g + 1)
                                after(act, s["m_hp"], g - 1)
                                act.activation(attr_t[u % 2][:], p_attr[u % 2][:], ACT.Copy).then_inc(s["m_attr"], 1)
                            if at := before(rnd, u, 1, tail):
                                g, q = at[0] * U + at[1], at[1]
                                after(act, s["m_sum"], g + 1)
                                after(act, s["m_aggp"], g - 1)
                                act.activation(hid[q % 2][:], pre[q % 2][:], ACT.Relu).then_inc(s["m_h"], 1)

                    rounds(act, NR, body, 1)
                with act.Else():
                    general_scalar(act)

            @block.vector
            def _(dve):
                with dve.If(is_fast(dve, k)):
                    for u in range(U):
                        dve.tensor_copy(r.idx[u][:], k.src_t[:, u, :]).then_inc(r.s_idx, 1)

                    def body(rnd, slots, tail):
                        for u in slots:
                            if not tail:
                                g = rnd * U + u
                                hold(dve, r.s_in[u], n_in * (rnd + 1))
                                hold(dve, s["m_hp"], g - 1)
                                hold(dve, s["m_aggp"], g - 3)
                                dve.tensor_scalar(hot_t[u % 2][:], r.row[u][:], k.win_id[:, bass.ds(g, 1)], None,
                                                  ALU.is_equal)
                                dve.scalar_tensor_tensor(
                                    out=hot[u % 4][:], in0=k.iota_w[:].unsqueeze(1).to_broadcast([P, J, W]),
                                    scalar=k.base[:, bass.ds(g, 1)],
                                    in1=k.dst_t[:, bass.ds(g, 1), :].rearrange("p a j -> p (a j)").unsqueeze(2)
                                    .to_broadcast([P, J, W]), op0=ALU.add, op1=ALU.is_equal).then_inc(s["m_masks"], 1)
                            if at := before(rnd, u, 1, tail):
                                g, q = at[0] * U + at[1], at[1]
                                hold(dve, s["m_hp"], g + 1)
                                hold(dve, r.s_got[q], 16 * J * (at[0] + 1))
                                hold(dve, s["m_h"], g - 1)
                                dve.tensor_tensor(pre[q % 2][:], p_hid[q % 2][:],
                                                  r.got[q][:].rearrange("p j d -> p (j d)"), ALU.add).then_inc(s["m_sum"], 1)
                                dve.tensor_copy(r.idx[q][:], k.src_t[:, bass.ds(g + U, 1), :].rearrange(
                                    "p a j -> p (a j)")).then_inc(r.s_idx, 1)
                            if at := before(rnd, u, 2, tail):
                                g, q = at[0] * U + at[1], at[1]
                                n0 = dve.value_load(k.base_i[0:1, bass.ds(g, 1)], min_val=0, max_val=k.NP - W)
                                hold(dve, s["m_aggp"], g + 1)
                                hold(dve, s["m_agg"], g)
                                dve.tensor_tensor(k.acc[:, :, bass.ds(n0, W)], k.acc[:, :, bass.ds(n0, W)],
                                                  p_agg[q % 2][:, 0:2 * W].rearrange("p (c w) -> p c w", c=2),
                                                  ALU.add).then_inc(s["m_agg"], 1)

                    rounds(dve, NR, body, 2)
                    dve.wait_ge(s["m_agg"], G)
                with dve.Else():
                    general_vector(dve)
        sems.clear()


def nodes_middle(nc, t, k):
    N2 = NTB * P
    halves = [slice(0, HALF), slice(HALF, N2)]
    with ExitStack() as ctx:
        sems = Sems(nc, ctx)
        s = sems.named("b_aggp b_agg b_up b_u b_updp b_y b_yt b_st b_var b_sd b_rs b_nm b_yn b_g b_bt b_x b_st2 "
                             "b_var2 b_sd2 b_rs2 b_nm2 b_h2 b_h2p b_h2t b_lzp b_num b_zb b_z b_esp b_es b_lrp b_lr "
                             "b_hi b_r b_mid b_lo b_out ")

        def sb(name, shape, dt=F32):
            return ctx.enter_context(nc.sbuf_tensor(name, shape, dt))

        agg = sb("b_aggT", [P, N2])
        ut = sb("b_uT", [P, N2])
        yt = sb("b_yT", [P, N2])
        st = sb("b_stats", [P, NTB, 6])
        mv = sb("b_mv", [P, NTB, 2])
        sd = sb("b_sdev", [P, NTB])
        rs = sb("b_rstd", [P, NTB])
        nm = sb("b_nmean", [P, NTB])
        st2 = sb("b_stats2", [P, NTB, 6])
        mv2 = sb("b_mv2", [P, NTB, 2])
        sd2 = sb("b_sdev2", [P, NTB])
        rs2 = sb("b_rstd2", [P, NTB])
        nm2 = sb("b_nmean2", [P, NTB])
        yn = sb("b_ynorm", [P, NTB, P])
        h2 = sb("b_hid2", [P, NTB, P])
        h2t = sb("b_h2T", [P, N2])
        zb = sb("b_zbias", [P, N2])
        zt = sb("b_zT", [P, N2])
        es = sb("b_selflog", [H, N2])
        lr = sb("b_lrrows", [P, NTB, 2, P])
        r1 = sb("b_rest", [P, NTB, P])
        r3 = [sb(f"b_part{q}", [P, NTB, P], BF16) for q in range(3)]

        def tile_of(first, q):
            return k.bank[first + q // 4][:, (q % 4) * P:(q % 4 + 1) * P]

        def both(buf):
            return [(buf[:, 0:512], 0, 512), (buf[:, 512:N2], 1, N2 - 512)]

        with nc.Block() as block:

            @block.tensor
            def _(pe):
                with pe.Fori(0, k.NI) as i:
                    for b, cols in enumerate(halves):
                        at = bass.ds(i * N2 + b * HALF, HALF)
                        pe.matmul(k.bank[b][:, 0:HALF], lhsT=k.w2[:], rhs=k.acc[:, 0, at], start=True, stop=False)
                        last = pe.matmul(k.bank[b][:, 0:HALF], lhsT=k.b2[:], rhs=k.acc[0:1, 1, at], start=False,
                                         stop=True)
                    last.then_inc(s["b_aggp"], 1)
                    hold(pe, s["b_agg"], i + 1)
                    for b, cols in enumerate(halves):
                        at = bass.ds(i * N2 + b * HALF, HALF)
                        pe.matmul(k.bank[2 + b][:, 0:HALF], lhsT=k.u1[:, 0, :], rhs=k.HT[:, at], start=True, stop=False)
                        last = pe.matmul(k.bank[2 + b][:, 0:HALF], lhsT=k.u1[:, 1, :], rhs=agg[:, cols], start=False,
                                         stop=True)
                    last.then_inc(s["b_up"], 1)
                    hold(pe, s["b_u"], i + 1)
                    for b, cols in enumerate(halves):
                        last = pe.matmul(k.bank[4 + b][:, 0:HALF], lhsT=k.u2[:], rhs=ut[:, cols], start=True, stop=True)
                    last.then_inc(s["b_updp"], 1)
                    hold(pe, s["b_y"], i + 1)
                    for q in range(NTB):
                        last = pe.transpose(tile_of(6, q), yt[:, q * P:(q + 1) * P], k.ident[:])
                    last.then_inc(s["b_yt"], 1)
                    hold(pe, s["b_h2"], i + 1)
                    for q in range(NTB):
                        last = pe.transpose(tile_of(0, q), h2[:, q, :], k.ident[:])
                    last.then_inc(s["b_h2p"], 1)
                    hold(pe, s["b_h2t"], i + 1)
                    for b, cols in enumerate(halves):
                        pe.matmul(k.bank[2 + b][:, 0:HALF], lhsT=k.wlr[:, 0, :], rhs=h2t[:, cols], start=True, stop=True)
                        pe.matmul(k.bank[4 + b][:, 0:HALF], lhsT=k.wlr[:, 0, :], rhs=h2t[:, cols], start=True,
                                  stop=False)
                        last = pe.matmul(k.bank[4 + b][:, 0:HALF], lhsT=k.wlr[:, 1, :], rhs=h2t[:, cols], start=False,
                                         stop=True)
                    last.then_inc(s["b_lzp"], 1)
                    hold(pe, s["b_z"], i + 1)
                    for b, cols in enumerate(halves):
                        last = pe.matmul(k.bank[6 + b][0:H, 0:HALF], lhsT=k.att4[:], rhs=zt[:, cols], start=True,
                                         stop=True)
                    last.then_inc(s["b_esp"], 1)
                    hold(pe, s["b_num"], i + 1)
                    for q in range(NTB):
                        last = pe.matmul(k.bank[q // 2][:, (q % 2) * 2 * P:(q % 2 + 1) * 2 * P],
                                         lhsT=h2t[:, q * P:(q + 1) * P], rhs=k.wlr[:].rearrange("p a d -> p (a d)"),
                                         start=True, stop=True)
                    last.then_inc(s["b_lrp"], 1)
                    hold(pe, s["b_lr"], i + 1)
                    hold(pe, s["b_es"], i + 1)

            @block.scalar
            def _(act):
                with act.Fori(0, k.NI) as i:
                    hold(act, s["b_aggp"], i + 1)
                    for b, cols in enumerate(halves):
                        last = act.activation(agg[:, cols], k.bank[b][:, 0:HALF], ACT.Copy)
                    last.then_inc(s["b_agg"], 1)
                    hold(act, s["b_up"], i + 1)
                    for b, cols in enumerate(halves):
                        last = act.activation(ut[:, cols], k.bank[2 + b][:, 0:HALF], ACT.Relu, bias=k.ub1[:, 0:1])
                    last.then_inc(s["b_u"], 1)
                    hold(act, s["b_var"], i + 1)
                    act.activation(sd[:], mv[:, :, 1], ACT.Sqrt, bias=k.eps[:, 0:1]).then_inc(s["b_sd"], 1)
                    hold(act, s["b_nm"], i + 1)
                    for q in range(NTB):
                        last = act.activation(yn[:, q, :], tile_of(6, q), ACT.Identity, scale=rs[:, q:q + 1],
                                              bias=nm[:, q:q + 1])
                    last.then_inc(s["b_yn"], 1)
                    hold(act, s["b_var2"], i + 1)
                    act.activation(sd2[:], mv2[:, :, 1], ACT.Sqrt, bias=k.eps[:, 0:1]).then_inc(s["b_sd2"], 1)
                    hold(act, s["b_nm2"], i + 1)
                    for q in range(NTB):
                        last = act.activation(h2[:, q, :], k.X[:, bass.ds(i * NTB + q, 1), :], ACT.Relu,
                                              scale=rs2[:, q:q + 1], bias=nm2[:, q:q + 1])
                    last.then_inc(s["b_h2"], 1)
                    hold(act, s["b_h2p"], i + 1)
                    for dst, b, n in both(h2t):
                        last = act.activation(dst, k.bank[b][:, 0:n], ACT.Copy)
                    last.then_inc(s["b_h2t"], 1)
                    hold(act, s["b_lzp"], i + 1)
                    for b, cols in enumerate(halves):
                        last = act.activation(zb[:, cols], k.bank[4 + b][:, 0:HALF], ACT.Identity, bias=k.blr[:, 0:1])
                    last.then_inc(s["b_zb"], 1)
                    for b, cols in enumerate(halves):
                        last = act.activation(k.acc[:, 0, bass.ds(i * N2 + b * HALF, HALF)], k.bank[2 + b][:, 0:HALF],
                                              ACT.Identity, bias=k.bl[:, 0:1])
                    last.then_inc(s["b_num"], 1)
                    hold(act, s["b_esp"], i + 1)
                    for b, cols in enumerate(halves):
                        last = act.activation(es[:, cols], k.bank[6 + b][0:H, 0:HALF], ACT.Copy)
                    last.then_inc(s["b_es"], 1)
                    hold(act, s["b_lr"], i + 1)
                    act.activation(r3[0][:], lr[:, :, 1, :], ACT.Copy).then_inc(s["b_hi"], 1)
                    hold(act, s["b_r"], i + 1)
                    act.activation(r3[1][:], r1[:], ACT.Copy).then_inc(s["b_mid"], 1)
                    hold(act, s["b_out"], (i + 1) * 16 * 6)

            @block.vector
            def _(dve):
                def norm_scale(var, sd_, rs_, nm_, s_sd, s_rs, s_nm, i):
                    hold(dve, s_sd, i + 1)
                    dve.reciprocal(rs_[:], sd_[:]).then_inc(s_rs, 1)
                    hold(dve, s_rs, i + 1)
                    dve.scalar_tensor_tensor(out=nm_[:], in0=var[:, :, 0], scalar=-1.0, in1=rs_[:], op0=ALU.mult,
                                             op1=ALU.mult).then_inc(s_nm, 1)

                with dve.Fori(0, k.NI) as i:
                    hold(dve, s["b_updp"], i + 1)
                    for b, cols in enumerate(halves):
                        last = dve.scalar_tensor_tensor(out=yt[:, cols], in0=k.bank[4 + b][:, 0:HALF],
                                                        scalar=k.ub2[:, 0:1],
                                                        in1=k.HT[:, bass.ds(i * N2 + b * HALF, HALF)],
                                                        op0=ALU.add, op1=ALU.add)
                    last.then_inc(s["b_y"], 1)
                    hold(dve, s["b_yt"], i + 1)
                    for q in range(NTB):
                        last = dve.bn_stats(st[:, q, :], tile_of(6, q))
                    last.then_inc(s["b_st"], 1)
                    hold(dve, s["b_st"], i + 1)
                    for q in range(NTB):
                        last = dve.bn_aggr(mv[:, q, :], st[:, q, :])
                    last.then_inc(s["b_var"], 1)
                    norm_scale(mv, sd, rs, nm, s["b_sd"], s["b_rs"], s["b_nm"], i)
                    hold(dve, s["b_yn"], i + 1)
                    dve.tensor_tensor(yn[:], yn[:], k.gamma_bc[:].unsqueeze(1).to_broadcast([P, NTB, P]), ALU.mult
                                      ).then_inc(s["b_g"], 1)
                    hold(dve, s["b_g"], i + 1)
                    dve.tensor_tensor(yn[:], yn[:], k.beta_bc[:].unsqueeze(1).to_broadcast([P, NTB, P]), ALU.add
                                      ).then_inc(s["b_bt"], 1)
                    hold(dve, s["b_bt"], i + 1)
                    xs = k.X[:, bass.ds(i * NTB, NTB), :]
                    dve.tensor_tensor(xs, xs, yn[:], ALU.add).then_inc(s["b_x"], 1)
                    hold(dve, s["b_x"], i + 1)
                    for q in range(NTB):
                        last = dve.bn_stats(st2[:, q, :], k.X[:, bass.ds(i * NTB + q, 1), :])
                    last.then_inc(s["b_st2"], 1)
                    hold(dve, s["b_st2"], i + 1)
                    for q in range(NTB):
                        last = dve.bn_aggr(mv2[:, q, :], st2[:, q, :])
                    last.then_inc(s["b_var2"], 1)
                    norm_scale(mv2, sd2, rs2, nm2, s["b_sd2"], s["b_rs2"], s["b_nm2"], i)
                    hold(dve, s["b_zb"], i + 1)
                    dve.scalar_tensor_tensor(out=zt[:], in0=zb[:], scalar=SLOPE, in1=zb[:], op0=ALU.mult,
                                             op1=ALU.max).then_inc(s["b_z"], 1)
                    hold(dve, s["b_lrp"], i + 1)
                    for b in range(4):
                        n = min(2, NTB - 2 * b)
                        last = dve.tensor_tensor(lr[:, 2 * b:2 * b + n],
                                                 k.bank[b][:, 0:n * 2 * P].rearrange("p (q a d) -> p q a d", a=2, d=P),
                                                 k.blr_bc[:].unsqueeze(1).to_broadcast([P, n, 2, P]), ALU.add)
                    last.then_inc(s["b_lr"], 1)
                    hold(dve, s["b_hi"], i + 1)
                    dve.tensor_tensor(r1[:], lr[:, :, 1, :], r3[0][:], ALU.subtract).then_inc(s["b_r"], 1)
                    hold(dve, s["b_mid"], i + 1)
                    dve.tensor_tensor(r3[2][:], r1[:], r3[1][:], ALU.subtract).then_inc(s["b_lo"], 1)
                    hold(dve, s["b_out"], (i + 1) * 16 * 6)

            @block.sync
            def _(sp):
                with sp.Fori(0, k.NI) as i:
                    hold(sp, s["b_es"], i + 1)
                    sp.dma_start(k.tab_es[:, bass.ds(i * N2, N2)], es[:]).then_inc(s["b_out"], 16)
                    hold(sp, s["b_lo"], i + 1)
                    store_tables(sp, s, k, s["b_out"], i * N2, [(k.tab_l, lr[:, :, 0, :]), (k.tab_r, lr[:, :, 1, :])],
                                 [(k.tab_r3, [b[:] for b in r3])])
                sp.wait_ge(s["b_out"], k.NI * 16 * 6)
        sems.clear()


def edges_attention(nc, t, k):
    G, NR = k.G, k.NR
    with ExitStack() as ctx:
        sems = Sems(nc, ctx)
        r = edge_slots(ctx, nc, sems, "t")
        s = sems.named("t_ones t_masks t_wide t_shift t_pen t_zp t_z02 t_z t_ep t_mg t_gone t_new t_pp t_mold t_max t_drop t_c t_cd "
                             "t_emp t_em t_w t_wx t_ndp t_sc t_acc ")

        def sb(name, shape, dt=F32):
            return ctx.enter_context(nc.sbuf_tensor("t_" + name, shape, dt))

        def ring(name, n, shape, dt=F32):
            return [sb(f"{name}{q}", shape, dt) for q in range(n)]

        self_in = ring("self_in", U, [P, 1])
        hot_t = ring("hot_t", 2, [P, EG], BF16)
        wide_t = ring("wide_t", 4, [P, EG])
        pen = ring("pen", 4, [P, EG])
        hot = ring("hot", U, [P, J, W])
        shift = ring("shift", 4, [P, P])
        z02 = ring("z02", 2, [P, EG])
        zt = ring("zt", 4, [P, EG])
        junk = sb("junk", [P, EG])
        mg = ring("mg", 2, [P, 1])
        prev = sb("prev", [P, 2])
        gone = sb("gone", [P, 1])
        mold = sb("mold", [P, 1])
        drop = sb("drop", [P, 1])
        c = sb("c", [P, 1])
        cd = sb("cd", [P, W])
        mneg = ring("mneg", 2, [P, H])
        em = ring("em", 2, [P, J, H])
        wt = ring("wt", 2, [P, J, H, W])
        wx = ring("wx", 2, [P, J, P])
        scaled = sb("scaled", [P, 2, W])
        p_z, p_e = k.bank[0:2], k.bank[2:4]
        p_em, p_prev, p_nd = k.bank[4], k.bank[5], k.bank[6:8]
        n_in = 16 * 5

        def load(sp, g, u):
            sp.dma_start(r.row[u][:], k.dst_rows[bass.ds(g, 1), :].to_broadcast([P, EG])).then_inc(r.s_in[u], 16)
            n0 = sp.value_load(k.base_i[0:1, bass.ds(g, 1)], min_val=0, max_val=k.NP - W)
            for part in range(3):
                sp.dma_start(r.win[u][part * W:(part + 1) * W, :], k.tab_r3[part, bass.ds(n0, W), :]
                             ).then_inc(r.s_in[u], 16)
            with nc.allow_non_contiguous_dma(reason="one logit on each partition"):
                sp.dma_start(self_in[u][:], k.tab_es[:, bass.ds(n0, W)]).then_inc(r.s_in[u], 16)

        gen = General(sems, k, "y", "in idx got m0 zp z02 z ep hot chain max drop c emp em w wx "
                                      "ndp acc group")
        y = gen.s
        ids = sb("y_ids", [P, 2, J], I32)
        got = [r.got[0], r.got[1]]
        top = sb("y_top", [P, k.NW])

        def general_sync(sp):
            with nc.allow_non_contiguous_dma(reason="turns the self logits, once"):
                for h in range(H):
                    sp.dma_start(top[h * W:(h + 1) * W, :], k.tab_es[h, :].rearrange("(w n) -> n w", n=W)
                                 ).then_inc(y["m0"], 16)

            def group(g):
                sp.dma_start(r.row[0][:], k.dst_rows[bass.ds(g, 1), :].to_broadcast([P, EG])).then_inc(y["in"], 16)
                hold(sp, y["acc"], (g + 1) * k.NW)

            gen.each_group(sp, group)

        def general_gpsimd(pool):
            gen.each_group(pool, lambda g: general_gathers(pool, ids, got, (k.tab_l, k.tab_r), y["idx"], y["got"],
                                                           y["group"], g))

        def general_tensor(pe):
            def group(g):
                hold(pe, y["got"], 16 * 2 * J * (g + 1))
                for j in range(J):
                    for v in range(2):
                        last = pe.matmul(p_z[0][:, j * P:(j + 1) * P], lhsT=got[v][:, j, :], rhs=k.ident[:],
                                         is_transpose=True, start=(v == 0), stop=(v == 1))
                last.then_inc(y["zp"], 1)
                hold(pe, y["z"], g + 1)
                pe.matmul(p_e[0][:], lhsT=k.att_w[:], rhs=zt[0][:], start=True, stop=True).then_inc(y["ep"], 1)

                def window(w, step):
                    hold(pe, y["max"], step + 1)
                    for j in range(J):
                        e = slice(j * P, (j + 1) * P)
                        pe.matmul(p_em[:, j * H:(j + 1) * H], lhsT=zt[0][:, e], rhs=k.att4[:], start=True, stop=False)
                        last = pe.matmul(p_em[:, j * H:(j + 1) * H], lhsT=wide_t[0][:, e], rhs=mneg[0][:],
                                         start=False, stop=True)
                    last.then_inc(y["emp"], 1)
                    hold(pe, y["wx"], step + 1)
                    for n, left in enumerate((wx[0][:], wt[0][:].rearrange("p j h c -> p j (h c)"))):
                        for j in range(J):
                            pe.matmul(p_nd[0][:, n * W:(n + 1) * W], lhsT=left[:, j, :], rhs=hot[0][:, j, :],
                                      start=(j == 0), stop=(j == J - 1))
                    pe.matmul(p_nd[0][:, 2 * W:3 * W], lhsT=k.same_head[:], rhs=cd[:], start=True, stop=True
                              ).then_inc(y["ndp"], 1)
                    hold(pe, y["acc"], step + 1)

                gen.each_window(pe, g, window)

            gen.each_group(pe, group)

        def general_scalar(act):
            def group(g):
                hold(act, y["zp"], g + 1)
                act.activation(z02[0][:], p_z[0][:], ACT.Copy, scale=SLOPE).then_inc(y["z02"], 1)

                def window(w, step):
                    hold(act, y["drop"], step + 1)
                    act.activation(c[:], drop[:], ACT.Exp).then_inc(y["c"], 1)
                    hold(act, y["em"], step + 1)
                    act.activation(wt[0][:].rearrange("p j h c -> p (j h) c"),
                                   em[0][:].rearrange("p j h -> p (j h)").unsqueeze(2).to_broadcast([P, J * H, W]),
                                   ACT.Exp).then_inc(y["w"], 1)

                gen.each_window(act, g, window)

            gen.each_group(act, group)

        def general_vector(dve):
            dve.memset(k.acc[:, 1, :], 1.0).then_inc(s["t_ones"], 1)
            dve.wait_ge(s["t_ones"], 1)
            dve.wait_ge(y["m0"], 16 * H)

            def group(g):
                general_indices(dve, k, Chain(dve, y["idx"], 2, g), ids, g)
                hold(dve, y["z02"], g + 1)
                dve.tensor_tensor(zt[0][:], p_z[0][:], z02[0][:], ALU.max).then_inc(y["z"], 1)
                hold(dve, y["ep"], g + 1)
                hold(dve, y["in"], 16 * (g + 1))

                def window(w, step):
                    chain = Chain(dve, y["chain"], 6, step)
                    m = top[:, bass.ds(w, 1)]
                    dve.tensor_scalar(wide_t[0][:], r.row[0][:], k.gen_win_id[:, bass.ds(w, 1)], None, ALU.is_equal)
                    general_hot(dve, k, hot[0], g, w)
                    chain.link(dve.tensor_scalar(pen[0][:], r.row[0][:], k.gen_win_id[:, bass.ds(w, 1)], -BIG,
                                                 ALU.not_equal, ALU.mult))
                    chain.link(dve.tensor_tensor_reduce(out=junk[:], in0=p_e[0][:], in1=pen[0][:], scale=1.0,
                                                        scalar=-3.0e38, op0=ALU.add, op1=ALU.max,
                                                        accum_out=mg[0][:]))
                    chain.link(dve.tensor_copy(mold[:], m))
                    chain.link(dve.tensor_tensor(prev[:, 0:1], mold[:], mg[0][:], ALU.max))
                    chain.link(dve.tensor_copy(m, prev[:, 0:1]))
                    dve.tensor_tensor(drop[:], mold[:], prev[:, 0:1], ALU.subtract).then_inc(y["drop"], 1)
                    dve.tensor_scalar(mneg[0][:], k.head4[:], prev[:, 0:1], -1.0, ALU.mult, ALU.mult
                                      ).then_inc(y["max"], 1)
                    hold(dve, y["c"], step + 1)
                    dve.tensor_scalar(cd[:], k.diag_w[:], c[:, 0:1], None, ALU.mult)
                    hold(dve, y["emp"], step + 1)
                    dve.tensor_scalar(em[0][:].rearrange("p j h -> p (j h)"), p_em[:, 0:J * H], 0.0, None, ALU.min
                                      ).then_inc(y["em"], 1)
                    hold(dve, y["w"], step + 1)
                    dve.tensor_tensor(wx[0][:], got[0][:], wt[0][:].rearrange("p j h c -> p j (h c)"), ALU.mult
                                      ).then_inc(y["wx"], 1)
                    hold(dve, y["ndp"], step + 1)
                    cols = k.acc[:, :, bass.ds(w * W, W)]
                    chain.link(dve.tensor_tensor(scaled[:], cols, p_nd[0][:, 2 * W:3 * W].unsqueeze(1)
                                                 .to_broadcast([P, 2, W]), ALU.mult))
                    dve.tensor_tensor(cols, scaled[:], p_nd[0][:, 0:2 * W].rearrange("p (c w) -> p c w", c=2), ALU.add
                                      ).then_inc(y["acc"], 1)
                    hold(dve, y["acc"], step + 1)
                    chain.done()

                gen.each_window(dve, g, window)
                dve.memset(gone[:], 0.0).then_inc(y["group"], 1)

            gen.each_group(dve, group)

        with nc.Block() as block:

            @block.sync
            def _(sp):
                with sp.If(is_fast(sp, k)):
                    for u in range(U):
                        load(sp, u, u)
                    with sp.Fori(1, NR) as rnd:
                        for u in range(U):
                            g = rnd * U + u
                            hold(sp, s["t_mold"], g + 1 - U)
                            hold(sp, s["t_zp"], g + 1 - U)
                            load(sp, g, u)
                with sp.Else():
                    general_sync(sp)

            @block.gpsimd
            def _(pool):
                with pool.If(is_fast(pool, k)):
                    gather_rounds(pool, k, r, k.tab_l, s["t_wx"])
                with pool.Else():
                    general_gpsimd(pool)

            @block.tensor
            def _(pe):
                with pe.If(is_fast(pe, k)):
                    def body(rnd, slots, tail):
                        for u in slots:
                            if at := before(rnd, u, 3, tail):
                                g, q = at[0] * U + at[1], at[1]
                                hold(pe, s["t_max"], g + 1)
                                hold(pe, s["t_wide"], g + 1)
                                hold(pe, s["t_em"], g)
                                for j in range(J):
                                    e = slice(j * P, (j + 1) * P)
                                    pe.matmul(p_em[:, j * H:(j + 1) * H], lhsT=zt[q % 4][:, e], rhs=k.att4[:],
                                              start=True, stop=False)
                                    last = pe.matmul(p_em[:, j * H:(j + 1) * H], lhsT=wide_t[q % 4][:, e],
                                                     rhs=mneg[q % 2][:], start=False, stop=True)
                                last.then_inc(s["t_emp"], 1)
                            if at := before(rnd, u, 2, tail):
                                g, q = at[0] * U + at[1], at[1]
                                hold(pe, s["t_shift"], g + 1)
                                hold(pe, s["t_max"], g)
                                if isinstance(g, int) and g == 0:
                                    pe.wait_ge(s["t_ones"], 1)
                                pe.matmul(p_prev[:, 0:2], lhsT=shift[q % 4][:], rhs=prev[:], start=True, stop=True
                                          ).then_inc(s["t_pp"], 1)
                            if at := before(rnd, u, 4, tail):
                                g, q = at[0] * U + at[1], at[1]
                                hold(pe, s["t_wx"], g + 1)
                                hold(pe, s["t_cd"], g + 1)
                                hold(pe, s["t_acc"], g - 1)
                                for n, left in enumerate((wx[q % 2][:], wt[q % 2][:].rearrange("p j h c -> p j (h c)"))):
                                    for j in range(J):
                                        pe.matmul(p_nd[q % 2][:, n * W:(n + 1) * W], lhsT=left[:, j, :],
                                                  rhs=hot[q % U][:, j, :], start=(j == 0), stop=(j == J - 1))
                                pe.matmul(p_nd[q % 2][:, 2 * W:3 * W], lhsT=k.same_head[:], rhs=cd[:], start=True,
                                          stop=True).then_inc(s["t_ndp"], 1)
                            if not tail:
                                g = rnd * U + u
                                hold(pe, s["t_masks"], g + 1)
                                hold(pe, r.s_got[u], 16 * J * (rnd + 1))
                                hold(pe, s["t_z"], g - 1)
                                for j in range(J):
                                    e = slice(j * P, (j + 1) * P)
                                    pe.matmul(p_z[u % 2][:, e], lhsT=r.win[u][:], rhs=hot_t[u % 2][0:3 * W, e],
                                              start=True, stop=False)
                                    last = pe.matmul(p_z[u % 2][:, e], lhsT=r.got[u][:, j, :], rhs=k.ident[:],
                                                     is_transpose=True, start=False, stop=True)
                                last.then_inc(s["t_zp"], 1)
                            if at := before(rnd, u, 1, tail):
                                g, q = at[0] * U + at[1], at[1]
                                hold(pe, s["t_z"], g + 1)
                                hold(pe, s["t_mg"], g - 1)
                                pe.matmul(p_e[q % 2][:], lhsT=k.att_w[:], rhs=zt[q % 4][:], start=True, stop=True
                                          ).then_inc(s["t_ep"], 1)

                    rounds(pe, NR, body, 4)
                with pe.Else():
                    general_tensor(pe)

            @block.scalar
            def _(act):
                with act.If(is_fast(act, k)):
                    def body(rnd, slots, tail):
                        for u in slots:
                            if at := before(rnd, u, 3, tail):
                                g, q = at[0] * U + at[1], at[1]
                                after(act, s["t_em"], g + 1)
                                after(act, s["t_ndp"], g - 1)
                                act.activation(wt[q % 2][:].rearrange("p j h c -> p (j h) c"),
                                               em[q % 2][:].rearrange("p j h -> p (j h)").unsqueeze(2)
                                               .to_broadcast([P, J * H, W]), ACT.Exp).then_inc(s["t_w"], 1)
                            if not tail:
                                g = rnd * U + u
                                after(act, s["t_masks"], g + 1)
                                after(act, s["t_emp"], g - 3)
                                act.activation(wide_t[u % 4][:], hot_t[u % 2][:], ACT.Copy).then_inc(s["t_wide"], 1)
                                after(act, s["t_zp"], g + 1)
                                after(act, s["t_z"], g - 1)
                                act.activation(z02[u % 2][:], p_z[u % 2][:], ACT.Copy, scale=SLOPE).then_inc(s["t_z02"], 1)
                            if at := before(rnd, u, 2, tail):
                                g, q = at[0] * U + at[1], at[1]
                                after(act, s["t_drop"], g + 1)
                                after(act, s["t_cd"], g)
                                act.activation(c[:], drop[:], ACT.Exp).then_inc(s["t_c"], 1)

                    rounds(act, NR, body, 3)
                with act.Else():
                    general_scalar(act)

            @block.vector
            def _(dve):
                with dve.If(is_fast(dve, k)):
                    dve.memset(k.acc[:, 1, :], 1.0)
                    dve.memset(prev[:], 1.0).then_inc(s["t_ones"], 1)
                    for u in range(U):
                        dve.tensor_copy(r.idx[u][:], k.src_t[:, u, :]).then_inc(r.s_idx, 1)
                    dve.wait_ge(s["t_ones"], 1)

                    def body(rnd, slots, tail):
                        for u in slots:
                            if at := before(rnd, u, 3, tail):
                                g, q = at[0] * U + at[1], at[1]
                                hold(dve, s["t_emp"], g + 1)
                                hold(dve, s["t_w"], g - 1)
                                dve.tensor_scalar(em[q % 2][:].rearrange("p j h -> p (j h)"), p_em[:, 0:J * H], 0.0, None,
                                                  ALU.min).then_inc(s["t_em"], 1)
                                hold(dve, s["t_c"], g + 1)
                                hold(dve, s["t_ndp"], g)
                                dve.tensor_scalar(cd[:], k.diag_w[:], c[:, 0:1], None, ALU.mult).then_inc(s["t_cd"], 1)
                            if not tail:
                                g = rnd * U + u
                                hold(dve, r.s_in[u], n_in * (rnd + 1))
                                hold(dve, s["t_zp"], g - 1)
                                hold(dve, s["t_wide"], g - 1)
                                dve.tensor_scalar(hot_t[u % 2][:], r.row[u][:], k.win_id[:, bass.ds(g, 1)], None,
                                                  ALU.is_equal).then_inc(s["t_masks"], 1)
                                hold(dve, s["t_mg"], g - 3)
                                dve.tensor_scalar(pen[u % 4][:], r.row[u][:], k.win_id[:, bass.ds(g, 1)], -BIG,
                                                  ALU.not_equal, ALU.mult).then_inc(s["t_pen"], 1)
                                hold(dve, s["t_ndp"], g + 1 - U)
                                dve.scalar_tensor_tensor(
                                    out=hot[u][:], in0=k.iota_w[:].unsqueeze(1).to_broadcast([P, J, W]),
                                    scalar=k.base[:, bass.ds(g, 1)],
                                    in1=k.dst_t[:, bass.ds(g, 1), :].rearrange("p a j -> p (a j)").unsqueeze(2)
                                    .to_broadcast([P, J, W]), op0=ALU.add, op1=ALU.is_equal)
                                hold(dve, s["t_pp"], g - 3)
                                dve.tensor_scalar(shift[u % 4][:], k.iota_c[:], k.shift_id[:, bass.ds(g, 1)], None,
                                                  ALU.is_equal).then_inc(s["t_shift"], 1)
                            if at := before(rnd, u, 1, tail):
                                g, q = at[0] * U + at[1], at[1]
                                hold(dve, s["t_z02"], g + 1)
                                hold(dve, s["t_emp"], g - 3)
                                dve.tensor_tensor(zt[q % 4][:], p_z[q % 2][:], z02[q % 2][:], ALU.max).then_inc(s["t_z"], 1)
                            if at := before(rnd, u, 3, tail):
                                g, q = at[0] * U + at[1], at[1]
                                hold(dve, s["t_w"], g + 1)
                                hold(dve, s["t_ndp"], g - 1)
                                dve.tensor_tensor(wx[q % 2][:], r.got[q][:], wt[q % 2][:].rearrange("p j h c -> p j (h c)"),
                                                  ALU.mult).then_inc(s["t_wx"], 1)
                                dve.tensor_copy(r.idx[q][:], k.src_t[:, bass.ds(g + U, 1), :].rearrange(
                                    "p a j -> p (a j)")).then_inc(r.s_idx, 1)
                            if at := before(rnd, u, 2, tail):
                                g, q = at[0] * U + at[1], at[1]
                                hold(dve, s["t_pp"], g + 1)
                                dve.tensor_scalar(gone[:], p_prev[:, 1:2], -1.0, BIG, ALU.add, ALU.mult
                                                  ).then_inc(s["t_gone"], 1)
                                hold(dve, s["t_ep"], g + 1)
                                dve.tensor_tensor_reduce(out=junk[:], in0=p_e[q % 2][:], in1=pen[q % 4][:], scale=1.0,
                                                         scalar=-3.0e38, op0=ALU.add, op1=ALU.max, accum_out=mg[q % 2][:]
                                                         ).then_inc(s["t_mg"], 1)
                                hold(dve, s["t_gone"], g + 1)
                                dve.scalar_tensor_tensor(out=mold[:], in0=p_prev[:, 0:1], scalar=gone[:, 0:1],
                                                         in1=self_in[q][:], op0=ALU.add, op1=ALU.max).then_inc(s["t_mold"], 1)
                                hold(dve, s["t_mold"], g + 1)
                                dve.tensor_tensor(prev[:, 0:1], mold[:], mg[q % 2][:], ALU.max).then_inc(s["t_new"], 1)
                                hold(dve, s["t_new"], g + 1)
                                hold(dve, s["t_c"], g)
                                dve.tensor_tensor(drop[:], mold[:], prev[:, 0:1], ALU.subtract).then_inc(s["t_drop"], 1)
                                dve.tensor_scalar(mneg[q % 2][:], k.head4[:], prev[:, 0:1], -1.0, ALU.mult, ALU.mult
                                                  ).then_inc(s["t_max"], 1)
                            if at := before(rnd, u, 4, tail):
                                g, q = at[0] * U + at[1], at[1]
                                n0 = dve.value_load(k.base_i[0:1, bass.ds(g, 1)], min_val=0, max_val=k.NP - W)
                                hold(dve, s["t_ndp"], g + 1)
                                hold(dve, s["t_acc"], g)
                                dve.tensor_tensor(scaled[:], k.acc[:, :, bass.ds(n0, W)],
                                                  p_nd[q % 2][:, 2 * W:3 * W].unsqueeze(1).to_broadcast([P, 2, W]),
                                                  ALU.mult).then_inc(s["t_sc"], 1)
                                hold(dve, s["t_sc"], g + 1)
                                dve.tensor_tensor(k.acc[:, :, bass.ds(n0, W)], scaled[:],
                                                  p_nd[q % 2][:, 0:2 * W].rearrange("p (c w) -> p c w", c=2),
                                                  ALU.add).then_inc(s["t_acc"], 1)

                    rounds(dve, NR, body, 4)
                    dve.wait_ge(s["t_acc"], G)
                with dve.Else():
                    general_vector(dve)
        sems.clear()


def nodes_last(nc, t, k):
    N2 = NTB * P
    tiles = k.N // P
    with ExitStack() as ctx:
        sems = Sems(nc, ctx)
        s = sems.named("c_den c_rec c_v c_neg c_bias c_exp c_elu c_tp c_o c_out c_rest ")

        def sb(name, shape):
            return ctx.enter_context(nc.sbuf_tensor("c_" + name, shape, F32))

        den = sb("den", [P, N2])
        rec = sb("rec", [P, N2])
        v = sb("v", [P, N2])
        vb = sb("vb", [P, N2])
        neg = sb("neg", [P, N2])
        ex = sb("ex", [P, N2])
        el = sb("el", [P, N2])
        o = sb("o", [P, NTB, P])
        with nc.Block() as block:

            @block.vector
            def _(dve):
                def step(i):
                    cols = bass.ds(i * N2, N2)
                    dve.tensor_scalar(den[:], k.acc[:, 1, cols], 1e-16, None, ALU.add).then_inc(s["c_den"], 1)
                    hold(dve, s["c_den"], i + 1)
                    dve.reciprocal(rec[:], den[:]).then_inc(s["c_rec"], 1)
                    hold(dve, s["c_rec"], i + 1)
                    dve.tensor_tensor(v[:], k.acc[:, 0, cols], rec[:], ALU.mult).then_inc(s["c_v"], 1)
                    hold(dve, s["c_v"], i + 1)
                    dve.tensor_scalar(neg[:], v[:], k.bias[:, 0:1], 0.0, ALU.add, ALU.min).then_inc(s["c_neg"], 1)
                    dve.tensor_scalar(vb[:], v[:], k.bias[:, 0:1], 0.0, ALU.add, ALU.max).then_inc(s["c_bias"], 1)
                    hold(dve, s["c_bias"], i + 1)
                    hold(dve, s["c_exp"], i + 1)
                    dve.scalar_tensor_tensor(out=el[:], in0=ex[:], scalar=-1.0, in1=vb[:], op0=ALU.add, op1=ALU.add
                                             ).then_inc(s["c_elu"], 1)
                    hold(dve, s["c_tp"], i + 1)
                    dve.tensor_tensor(o[:, 0:4, :], k.bank[0][:].rearrange("p (q d) -> p q d", d=P),
                                      k.X[:, bass.ds(i * NTB, 4), :], ALU.add)
                    dve.tensor_tensor(o[:, 4:NTB, :], k.bank[1][:, 0:(NTB - 4) * P].rearrange("p (q d) -> p q d", d=P),
                                      k.X[:, bass.ds(i * NTB + 4, NTB - 4), :], ALU.add).then_inc(s["c_o"], 1)

                with dve.Fori(0, k.NI - 1) as i:
                    step(i)
                    hold(dve, s["c_out"], 16 * (i + 1))
                step(k.NI - 1)

            @block.scalar
            def _(act):
                with act.Fori(0, k.NI) as i:
                    hold(act, s["c_neg"], i + 1)
                    act.activation(ex[:], neg[:], ACT.Exp).then_inc(s["c_exp"], 1)

            @block.tensor
            def _(pe):
                with pe.Fori(0, k.NI) as i:
                    hold(pe, s["c_elu"], i + 1)
                    for q in range(NTB):
                        last = pe.transpose(k.bank[q // 4][:, (q % 4) * P:(q % 4 + 1) * P], el[:, q * P:(q + 1) * P],
                                            k.ident[:])
                    last.then_inc(s["c_tp"], 1)
                    hold(pe, s["c_o"], i + 1)

            @block.sync
            def _(sp):
                with sp.Fori(0, k.NI - 1) as i:
                    hold(sp, s["c_o"], i + 1)
                    sp.dma_start(t["out"][bass.ds(i * N2, N2), :].rearrange("(t p) d -> p t d", p=P), o[:]
                                 ).then_inc(s["c_out"], 16)
                sp.wait_ge(s["c_o"], k.NI)
                first = (k.NI - 1) * NTB
                n = tiles - first
                if n:
                    sp.dma_start(t["out"][first * P:tiles * P, :].rearrange("(t p) d -> p t d", p=P), o[:, 0:n, :]
                                 ).then_inc(s["c_rest"], 16)
                if k.LAST:
                    sp.dma_start(t["out"][tiles * P:k.N, :], o[0:k.LAST, n, :]).then_inc(s["c_rest"], 16)
                sp.wait_ge(s["c_out"], 16 * (k.NI - 1))
                sp.wait_ge(s["c_rest"], 16 * (bool(n) + bool(k.LAST)))


_INS = ['x', 'src', 'dst', 'edge_attr_128', 'L0_gnn_msg_W1', 'L0_gnn_msg_b1', 'L0_gnn_msg_W2', 'L0_gnn_msg_b2',
        'L0_gnn_upd_W1', 'L0_gnn_upd_b1', 'L0_gnn_upd_W2', 'L0_gnn_upd_b2', 'L0_gnn_ln_gamma', 'L0_gnn_ln_beta',
        'L1_gnn_W_l', 'L1_gnn_b_l', 'L1_gnn_W_r', 'L1_gnn_b_r', 'L1_gnn_att', 'L1_gnn_bias']


def kernel(**inputs):
    import numpy as _np
    import concourse.bacc as _bacc
    from concourse import mybir as _mybir
    from concourse.bass_utils import run_bass_kernel_spmd as _run

    nc = _bacc.Bacc("TRN2", target_bir_lowering=False, num_devices=1)
    arrays, args = {}, {}
    for name in _INS:
        a = _np.ascontiguousarray(inputs[name])
        arrays[f"in_{name}_dram"] = a
        args[name] = nc.dram_tensor(f"in_{name}_dram", a.shape, _mybir.dt.from_np(a.dtype), kind="ExternalInput").ap()
    args["out"] = nc.dram_tensor("out_0_dram", inputs["x"].shape, _mybir.dt.float32, kind="ExternalOutput").ap()
    gnn_program(nc, args)
    r = _run(nc, [arrays], core_ids=[0])
    return r.results[0]["out_0_dram"]
```
